# Optimizing a Trainium2 kernel written in Bass

```python
import numpy as np
import jax
import jax.numpy as jnp

def _softmax(x, axis=-1):
    return jax.nn.softmax(x, axis=axis)

def _gelu(x):
    return jax.nn.gelu(x, approximate=True)

def _silu(x):
    return jax.nn.silu(x)

def _sigmoid(x):
    return jax.nn.sigmoid(x)

def _layernorm(x, axis=-1, eps=1e-05):
    m = jnp.mean(x, axis=axis, keepdims=True)
    v = jnp.var(x, axis=axis, keepdims=True)
    return (x - m) / jnp.sqrt(v + eps)

def _scatter_add(tgt, idx, src, axis=0):
    return tgt.at[idx].add(src)

def _segment_sum(src, seg, n):
    return jax.ops.segment_sum(src, seg, n)
kernel_name = 'mk_dlrm_tower_d1_rec_r8_754774'

def setup_inputs(seed: int=0):
    np.random.seed(seed)
    _w = jnp.asarray

    def _rec_inputs():
        import jax
        import jax.numpy as jnp
        _tk = jax.random.key(seed)
        dense_ctx = jax.random.normal(jax.random.fold_in(_tk, 190), (512, 16), jnp.float32)
        ids = jnp.stack([jax.random.randint(jax.random.fold_in(_tk, 200 + f), (512,), 0, v, jnp.int32) for f, v in enumerate([1250, 1000, 12500, 1250, 125000, 1000, 12500, 1000, 1000, 1250, 1000, 12500, 12500, 12500, 12500, 1250, 1000, 1000, 1250, 12500, 12500, 1250, 1250, 1250, 1250, 1000, 1250])], axis=1)
        tbl_0 = 0.05 * jax.random.normal(jax.random.fold_in(_tk, 500 + 0), (1250, 128), jnp.float32)
        tbl_1 = 0.05 * jax.random.normal(jax.random.fold_in(_tk, 500 + 1), (1000, 128), jnp.float32)
        tbl_2 = 0.05 * jax.random.normal(jax.random.fold_in(_tk, 500 + 2), (12500, 128), jnp.float32)
        tbl_3 = 0.05 * jax.random.normal(jax.random.fold_in(_tk, 500 + 3), (1250, 128), jnp.float32)
        tbl_4 = 0.05 * jax.random.normal(jax.random.fold_in(_tk, 500 + 4), (125000, 128), jnp.float32)
        tbl_5 = 0.05 * jax.random.normal(jax.random.fold_in(_tk, 500 + 5), (1000, 128), jnp.float32)
        tbl_6 = 0.05 * jax.random.normal(jax.random.fold_in(_tk, 500 + 6), (12500, 128), jnp.float32)
        tbl_7 = 0.05 * jax.random.normal(jax.random.fold_in(_tk, 500 + 7), (1000, 128), jnp.float32)
        tbl_8 = 0.05 * jax.random.normal(jax.random.fold_in(_tk, 500 + 8), (1000, 128), jnp.float32)
        tbl_9 = 0.05 * jax.random.normal(jax.random.fold_in(_tk, 500 + 9), (1250, 128), jnp.float32)
        tbl_10 = 0.05 * jax.random.normal(jax.random.fold_in(_tk, 500 + 10), (1000, 128), jnp.float32)
        tbl_11 = 0.05 * jax.random.normal(jax.random.fold_in(_tk, 500 + 11), (12500, 128), jnp.float32)
        tbl_12 = 0.05 * jax.random.normal(jax.random.fold_in(_tk, 500 + 12), (12500, 128), jnp.float32)
        tbl_13 = 0.05 * jax.random.normal(jax.random.fold_in(_tk, 500 + 13), (12500, 128), jnp.float32)
        tbl_14 = 0.05 * jax.random.normal(jax.random.fold_in(_tk, 500 + 14), (12500, 128), jnp.float32)
        tbl_15 = 0.05 * jax.random.normal(jax.random.fold_in(_tk, 500 + 15), (1250, 128), jnp.float32)
        tbl_16 = 0.05 * jax.random.normal(jax.random.fold_in(_tk, 500 + 16), (1000, 128), jnp.float32)
        tbl_17 = 0.05 * jax.random.normal(jax.random.fold_in(_tk, 500 + 17), (1000, 128), jnp.float32)
        tbl_18 = 0.05 * jax.random.normal(jax.random.fold_in(_tk, 500 + 18), (1250, 128), jnp.float32)
        tbl_19 = 0.05 * jax.random.normal(jax.random.fold_in(_tk, 500 + 19), (12500, 128), jnp.float32)
        tbl_20 = 0.05 * jax.random.normal(jax.random.fold_in(_tk, 500 + 20), (12500, 128), jnp.float32)
        tbl_21 = 0.05 * jax.random.normal(jax.random.fold_in(_tk, 500 + 21), (1250, 128), jnp.float32)
        tbl_22 = 0.05 * jax.random.normal(jax.random.fold_in(_tk, 500 + 22), (1250, 128), jnp.float32)
        tbl_23 = 0.05 * jax.random.normal(jax.random.fold_in(_tk, 500 + 23), (1250, 128), jnp.float32)
        tbl_24 = 0.05 * jax.random.normal(jax.random.fold_in(_tk, 500 + 24), (1250, 128), jnp.float32)
        tbl_25 = 0.05 * jax.random.normal(jax.random.fold_in(_tk, 500 + 25), (1000, 128), jnp.float32)
        tbl_26 = 0.05 * jax.random.normal(jax.random.fold_in(_tk, 500 + 26), (1250, 128), jnp.float32)
        _rk = jax.random.fold_in(_tk, 7)
        W_top1 = 0.0521996 * jax.random.normal(jax.random.fold_in(_tk, 801), (367, 512), jnp.float32)
        W_top2 = 0.0441942 * jax.random.normal(jax.random.fold_in(_tk, 802), (512, 256), jnp.float32)
        W_top3 = 0.0625 * jax.random.normal(jax.random.fold_in(_tk, 803), (256, 1), jnp.float32)
        b_top1 = jnp.zeros((512,), jnp.float32)
        b_top2 = jnp.zeros((256,), jnp.float32)
        return (dense_ctx, ids, tbl_0, tbl_1, tbl_2, tbl_3, tbl_4, tbl_5, tbl_6, tbl_7, tbl_8, tbl_9, tbl_10, tbl_11, tbl_12, tbl_13, tbl_14, tbl_15, tbl_16, tbl_17, tbl_18, tbl_19, tbl_20, tbl_21, tbl_22, tbl_23, tbl_24, tbl_25, tbl_26, W_top1, b_top1, W_top2, b_top2, W_top3)
    dense_ctx, ids, tbl_0, tbl_1, tbl_2, tbl_3, tbl_4, tbl_5, tbl_6, tbl_7, tbl_8, tbl_9, tbl_10, tbl_11, tbl_12, tbl_13, tbl_14, tbl_15, tbl_16, tbl_17, tbl_18, tbl_19, tbl_20, tbl_21, tbl_22, tbl_23, tbl_24, tbl_25, tbl_26, W_top1, b_top1, W_top2, b_top2, W_top3 = _rec_inputs()

    def _L0_rec_setup():
        import jax, jax.numpy as jnp
        import numpy as np

        def _tri_indices(num_feas):
            return np.array([i * num_feas + j for j in range(1, num_feas) for i in range(j)], dtype=np.int32)
        key = jax.random.key(seed)
        batch, num_feas, embed_dim = (2048, 27, 128)
        inputs = jax.random.normal(key, (batch, num_feas, embed_dim), dtype=jnp.float32)
        return {'inputs': inputs, 'num_feas': num_feas}
    _L0_rec_all = _L0_rec_setup()
    _L0_rec_in = {k: v for k, v in _L0_rec_all.items() if k in ()}
    del _L0_rec_all
    return {'dense_ctx': dense_ctx, 'ids': ids, 'tbl_0': tbl_0, 'tbl_1': tbl_1, 'tbl_2': tbl_2, 'tbl_3': tbl_3, 'tbl_4': tbl_4, 'tbl_5': tbl_5, 'tbl_6': tbl_6, 'tbl_7': tbl_7, 'tbl_8': tbl_8, 'tbl_9': tbl_9, 'tbl_10': tbl_10, 'tbl_11': tbl_11, 'tbl_12': tbl_12, 'tbl_13': tbl_13, 'tbl_14': tbl_14, 'tbl_15': tbl_15, 'tbl_16': tbl_16, 'tbl_17': tbl_17, 'tbl_18': tbl_18, 'tbl_19': tbl_19, 'tbl_20': tbl_20, 'tbl_21': tbl_21, 'tbl_22': tbl_22, 'tbl_23': tbl_23, 'tbl_24': tbl_24, 'tbl_25': tbl_25, 'tbl_26': tbl_26, 'W_top1': W_top1, 'b_top1': b_top1, 'W_top2': W_top2, 'b_top2': b_top2, 'W_top3': W_top3}

def reference(dense_ctx, ids, tbl_0, tbl_1, tbl_2, tbl_3, tbl_4, tbl_5, tbl_6, tbl_7, tbl_8, tbl_9, tbl_10, tbl_11, tbl_12, tbl_13, tbl_14, tbl_15, tbl_16, tbl_17, tbl_18, tbl_19, tbl_20, tbl_21, tbl_22, tbl_23, tbl_24, tbl_25, tbl_26, W_top1, b_top1, W_top2, b_top2, W_top3):
    import jax
    import jax.numpy as jnp

    def _L0_rec_ref(inputs, num_feas):
        import jax, jax.numpy as jnp
        import numpy as np

        def _tri_indices(num_feas):
            return np.array([i * num_feas + j for j in range(1, num_feas) for i in range(j)], dtype=np.int32)
        dot = jnp.einsum('bnd,bmd->bnm', inputs, inputs)
        idx = jnp.asarray(_tri_indices(num_feas))
        flat = dot.reshape(inputs.shape[0], num_feas * num_feas)
        return flat[:, idx]
    e = jnp.stack([tbl_0[ids[:, 0]], tbl_1[ids[:, 1]], tbl_2[ids[:, 2]], tbl_3[ids[:, 3]], tbl_4[ids[:, 4]], tbl_5[ids[:, 5]], tbl_6[ids[:, 6]], tbl_7[ids[:, 7]], tbl_8[ids[:, 8]], tbl_9[ids[:, 9]], tbl_10[ids[:, 10]], tbl_11[ids[:, 11]], tbl_12[ids[:, 12]], tbl_13[ids[:, 13]], tbl_14[ids[:, 14]], tbl_15[ids[:, 15]], tbl_16[ids[:, 16]], tbl_17[ids[:, 17]], tbl_18[ids[:, 18]], tbl_19[ids[:, 19]], tbl_20[ids[:, 20]], tbl_21[ids[:, 21]], tbl_22[ids[:, 22]], tbl_23[ids[:, 23]], tbl_24[ids[:, 24]], tbl_25[ids[:, 25]], tbl_26[ids[:, 26]]], axis=1)
    z = _L0_rec_ref(e, 27)
    z = z.reshape(z.shape[0], -1)
    h = jnp.concatenate([z, dense_ctx], axis=1)
    h = jnp.maximum(h @ W_top1 + b_top1, 0.0)
    h = jnp.maximum(h @ W_top2 + b_top2, 0.0)
    y = h @ W_top3
    return y

_drawn_inputs = setup_inputs


def setup_inputs(seed=0):
    import zlib

    import numpy as np

    out = dict(_drawn_inputs(seed))
    spreads = {'b_top1': (0.0, 0.1), 'b_top2': (0.0, 0.1)}
    factors = {}
    for name, (base, spread) in spreads.items():
        noise = np.random.default_rng([zlib.crc32(name.encode()), seed]).standard_normal(out[name].shape)
        drawn = base * np.exp(spread * noise) if base else spread * noise
        out[name] = jnp.asarray(drawn.astype(out[name].dtype))
    for name, factor in factors.items():
        out[name] = (out[name] * factor).astype(out[name].dtype)
    return out
```

```python
from contextlib import ExitStack

import concourse.bass as bass
import concourse.mybir as mybir
import numpy as np

FP32 = mybir.dt.float32
FP32R = mybir.dt.float32r
INT32 = mybir.dt.int32
ALU = mybir.AluOpType
ACT = mybir.ActivationFunctionType

P = 128
BATCH = 512
DIM = 128
ROWS = [1250, 1000, 12500, 1250, 125000, 1000, 12500, 1000, 1000, 1250, 1000, 12500, 12500, 12500,
        12500, 1250, 1000, 1000, 1250, 12500, 12500, 1250, 1250, 1250, 1250, 1000, 1250]
NF = len(ROWS)
DENSE = 16
H1, H2 = 512, 256
TILES = BATCH // P

CHUNK = 125
SELECTED = sorted(sorted(range(NF), key=lambda f: (ROWS[f], f))[:9], key=lambda f: (ROWS[f], f))
LOOKED_UP = [f for f in range(NF) if f not in SELECTED]
SLOTS = LOOKED_UP + SELECTED
NS, NL = len(SELECTED), len(LOOKED_UP)
CHUNKS = [ROWS[f] // CHUNK for f in SELECTED]
MAX_CHUNKS = max(CHUNKS)
FIRST_CHUNK = [sum(CHUNKS[:k]) for k in range(NS + 1)]
PER_BANK = 4
LOOKUP_GROUPS = [list(range(g, min(g + PER_BANK, NL))) for g in range(0, NL, PER_BANK)]
NG = len(LOOKUP_GROUPS)

QUAD = 32
SIDE = P // QUAD
GROUPS = P // SIDE
STEP_GROUPS = 8
STEPS = GROUPS // STEP_GROUPS

WIDTH = 4


def pack_plan():
    copies, pairs = [], []
    blocks = range(1, NF, WIDTH)
    for b0 in blocks:
        rows = min(WIDTH, NF - b0)
        copies.append((b0 * QUAD, QUAD, rows, b0))
        pairs += [(a, b) for b in range(b0, b0 + rows) for a in range(b0)]
    for r in range(1, WIDTH):
        inner = [b0 for b0 in blocks if b0 + r < NF]
        copies.append(((1 + r) * QUAD + 1, WIDTH * (QUAD + 1), len(inner), r))
        pairs += [(b0 + x, b0 + r) for b0 in inner for x in range(r)]
    return copies, pairs


COPIES, PAIRS = pack_plan()
NPAIRS = NF * (NF - 1) // 2
FEATURES = NPAIRS + DENSE
K1 = -(-FEATURES // P)
K2, K3 = H1 // P, H2 // P
ROOM = max(first + step * count for first, step, count, _ in COPIES)

ONEHOT_RING = 10
TABLE_RING = 2
IDS_RING = 3
FEED_RING = 2


def feature_rows():
    at = []
    for a, b in PAIRS:
        i, j = sorted((SLOTS[a], SLOTS[b]))
        at.append(j * (j - 1) // 2 + i)
    return at + list(range(NPAIRS, FEATURES))


def schedule():
    order = []
    early = [("transpose", t, g) for t in range(TILES) for g in range(NG)]
    for k in range(NS):
        order.append(("select", k))
        if k >= 2:
            order.append(early.pop(0))
    def rest(t):
        while early and early[0][1] <= t:
            order.append(early.pop(0))
    rest(0)
    order += [("gram", 0, c) for c in range(STEPS)]
    for t in range(1, TILES):
        rest(t)
        for c, stage in enumerate(("features", "layer1", "layer2", "layer3")):
            order.append(("gram", t, c))
            order.append((stage, t - 1))
    for stage in ("features", "layer1", "layer2", "layer3"):
        order.append((stage, TILES - 1))
    return order


SCHEDULE = schedule()
FEED = {step: n for n, step in enumerate(s for s in SCHEDULE if s[0] in ("select", "transpose"))}


def tower(nc, dense, ids, ids_rows, tables, w1, b1, w2, b2, w3, out):
    with ExitStack() as ctx:
        def sb(name, shape, dt=FP32):
            return ctx.enter_context(nc.sbuf_tensor(name, shape, dt))

        def ps(name, shape):
            return ctx.enter_context(nc.psum_tensor(name, shape, FP32))

        def sem(name):
            return ctx.enter_context(nc.semaphore(name))

        ids_sb = sb("ids_sb", [P, TILES, NF], INT32)
        rows_sb = sb("rows_sb", [P, TILES, NL, DIM])
        ids_all = sb("ids_all", [CHUNK, IDS_RING, BATCH], INT32)
        raw = sb("raw", [CHUNK, TABLE_RING, MAX_CHUNKS * DIM])
        hi = sb("hi", [CHUNK, TABLE_RING, MAX_CHUNKS * DIM], FP32R)
        lo = sb("lo", [CHUNK, TABLE_RING, MAX_CHUNKS * DIM], FP32R)
        onehot = sb("onehot", [CHUNK, ONEHOT_RING, BATCH], FP32R)
        number_i = sb("number_i", [CHUNK, 2, MAX_CHUNKS], INT32)
        number = sb("number", [CHUNK, 2, MAX_CHUNKS])
        embT = sb("embT", [P, TILES, GROUPS, SIDE, QUAD])
        identity = sb("identity", [P, P])
        blocks = sb("blocks", [P, GROUPS, NF])
        square = sb("square", [P, ROOM])
        feats = sb("feats", [P, 2, K1 * P])
        featsT = sb("featsT", [P, K1 * P])
        h1T = sb("h1T", [P, K2 * P])
        h2T = sb("h2T", [P, K3 * P])
        y_sb = sb("y_sb", [1, BATCH])
        w1_sb = sb("w1_sb", [P, K1, H1])
        w2_sb = sb("w2_sb", [P, K2, H2])
        w3_sb = sb("w3_sb", [P, K3])
        b1_sb = sb("b1_sb", [P, K2])
        b2_sb = sb("b2_sb", [P, K3])

        feed = ps("feed", [P, FEED_RING, BATCH])
        gram = ps("gram", [P, 2, 2, BATCH])
        mlp_a = ps("mlp_a", [P, BATCH])
        mlp_b = ps("mlp_b", [P, BATCH])

        ids_in = sem("ids_in")
        gathered = [[sem(f"gathered_{t}_{g}") for g in range(NG)] for t in range(TILES)]
        table_in = [sem(f"table_in_{r}") for r in range(TABLE_RING)]
        ids_all_in = [sem(f"ids_all_in_{r}") for r in range(IDS_RING)]
        w_in = sem("w_in")
        dense_in = [sem(f"dense_in_{t}") for t in range(2)]
        out_done = sem("out_done")
        setup = sem("setup")
        number_done = sem("number_done")
        pad_done = sem("pad_done")
        hi_done = sem("hi_done")
        lo_done = sem("lo_done")
        onehot_done = sem("onehot_done")
        chunk_used = sem("chunk_used")
        transposed = sem("transposed")
        feed_read = sem("feed_read")
        gram_full = sem("gram_full")
        blocks_done = sem("blocks_done")
        square_done = sem("square_done")
        packed = sem("packed")
        featsT_full = sem("featsT_full")
        featsT_done = sem("featsT_done")
        l1_full = sem("l1_full")
        h1_done = sem("h1_done")
        l2_full = sem("l2_full")
        h2_done = sem("h2_done")
        l3_full = sem("l3_full")
        y_done = sem("y_done")

        block = ctx.enter_context(nc.Block())

        @block.sync
        def _(sp):
            sp.dma_start(ids_sb[:, :, :], ids.rearrange("(t p) f -> p t f", p=P)).then_inc(ids_in, 16)

            def load_selected(k):
                f, n = SELECTED[k], CHUNKS[k]
                if k >= IDS_RING:
                    sp.wait_ge(onehot_done, FIRST_CHUNK[k - IDS_RING + 1])
                sp.dma_start(ids_all[:, k % IDS_RING, :],
                             ids_rows[f:f + 1, :].broadcast_to([CHUNK, BATCH])).then_inc(ids_all_in[k % IDS_RING], 16)
                if k >= TABLE_RING:
                    sp.wait_ge(hi_done, k - TABLE_RING + 1)
                    sp.wait_ge(lo_done, k - TABLE_RING + 1)
                sp.dma_start(raw[:, k % TABLE_RING, 0:n * DIM],
                             tables[f].rearrange("(p c) d -> p (c d)", c=n)).then_inc(table_in[k % TABLE_RING], 16)

            load_selected(0)
            load_selected(1)
            sp.dma_start(w1_sb[:, :, :], w1.rearrange("(k p) n -> p k n", p=P)).then_inc(w_in, 16)
            sp.dma_start(w2_sb[:, :, :], w2.rearrange("(k p) n -> p k n", p=P)).then_inc(w_in, 16)
            for dst, src in ((w3_sb, w3), (b1_sb, b1), (b2_sb, b2)):
                sp.dma_start(dst[:, :], src).then_inc(w_in, 16)

            def load_dense(t):
                if t >= 2:
                    sp.wait_ge(featsT_full, t - 1)
                sp.dma_start(feats[:, t % 2, NPAIRS:FEATURES], dense[t * P:(t + 1) * P, :]).then_inc(dense_in[t % 2], 16)

            load_dense(0)
            load_dense(1)
            for k in range(2, NS):
                load_selected(k)
            load_dense(2)
            load_dense(3)
            sp.wait_ge(y_done, TILES)
            sp.dma_start(out.rearrange("n o -> o n"), y_sb[:, :]).then_inc(out_done, 16)
            sp.wait_ge(out_done, 16)

        @block.gpsimd
        def _(pool):
            for n, chunks in enumerate(sorted(set(CHUNKS))):
                pool.iota(number_i[:, n, 0:chunks], pattern=[[1, chunks]], base=0,
                          channel_multiplier=chunks).then_inc(setup, 1)
            pool.memset(identity[:, :], 0.0).then_inc(setup, 1)
            constants = len(set(CHUNKS)) + 1
            pool.wait_ge(setup, constants)
            pool.affine_select(out=identity[:, :], in_=identity[:, :], compare_op=ALU.not_equal, fill=1.0,
                               base=0, pattern=[[-1, P]], channel_multiplier=1).then_inc(setup, 1)
            pool.wait_ge(ids_in, 16)
            for t in range(TILES):
                for g, group in enumerate(LOOKUP_GROUPS):
                    for n in group:
                        f = LOOKED_UP[n]
                        pool.indirect_dma_start(
                            rows_sb[:, t, n, :], None, tables[f],
                            bass.IndirectOffsetOnAxis(ap=ids_sb[:, t, f:f + 1], axis=0),
                        ).then_inc(gathered[t][g], 16)

        SETUP = len(set(CHUNKS)) + 2

        @block.scalar
        def _(act):
            def split_hi(k):
                n, r = CHUNKS[k], k % TABLE_RING
                act.wait_ge(table_in[r], 16 * (k // TABLE_RING + 1))
                if k >= TABLE_RING:
                    act.wait_ge(chunk_used, FIRST_CHUNK[k - TABLE_RING + 1])
                    act.wait_ge(lo_done, k - TABLE_RING + 1)
                act.activation(hi[:, r, 0:n * DIM], raw[:, r, 0:n * DIM], ACT.Copy).then_inc(hi_done, 1)

            def read_feed(step):
                n = FEED[step]
                bank = feed[:, n % FEED_RING, :]
                if step[0] == "select":
                    act.wait_ge(chunk_used, FIRST_CHUNK[step[1] + 1])
                    act.activation(embT[:, :, :, :, NL + step[1]].rearrange("p t g s -> p t s g"),
                                   bank.rearrange("p (t s g) -> p t s g", t=TILES, s=SIDE),
                                   ACT.Copy).then_inc(feed_read, 1)
                else:
                    _, t, g = step
                    group = LOOKUP_GROUPS[g]
                    act.wait_ge(transposed, t * NG + g + 1)
                    act.activation(embT[:, t, :, :, group[0]:group[-1] + 1].rearrange("p g s f -> p f s g"),
                                   bank[:, 0:len(group) * P].rearrange("p (f s g) -> p f s g", s=SIDE, g=GROUPS),
                                   ACT.Copy).then_inc(feed_read, 1)

            split_hi(0)
            split_hi(1)
            for step in SCHEDULE:
                if step[0] == "select":
                    read_feed(step)
                    if step[1] + 2 < NS:
                        split_hi(step[1] + 2)
                elif step[0] == "transpose":
                    read_feed(step)
                elif step[0] == "gram":
                    _, t, c = step
                    n = t * STEPS + c
                    act.wait_ge(gram_full, n + 1)
                    if t and c == 0:
                        act.wait_ge(square_done, t)
                    for q in range(SIDE):
                        rows = slice(q * QUAD, (q + 1) * QUAD)
                        g0 = c * STEP_GROUPS
                        src = gram[rows, n % 2, :, 0:4 * SIDE * NF].rearrange("p b (g m) -> p b g m", g=4)
                        act.activation(
                            blocks[rows, g0:g0 + STEP_GROUPS, :].rearrange("p (b g) f -> p b g f", b=2),
                            src[:, :, :, q * NF:(q + 1) * NF], ACT.Copy).then_inc(blocks_done, 1)
                elif step[0] == "layer1":
                    t = step[1]
                    act.wait_ge(w_in, 16 * 5)
                    if t:
                        act.wait_ge(l2_full, t)
                    act.wait_ge(l1_full, t + 1)
                    for m in range(K2):
                        act.activation(h1T[:, m * P:(m + 1) * P], mlp_b[:, m * P:(m + 1) * P], ACT.Relu,
                                       bias=b1_sb[:, m:m + 1]).then_inc(h1_done, 1)
                elif step[0] == "layer2":
                    t = step[1]
                    if t:
                        act.wait_ge(l3_full, t)
                    act.wait_ge(l2_full, t + 1)
                    for m in range(K3):
                        act.activation(h2T[:, m * P:(m + 1) * P], mlp_a[:, m * P:(m + 1) * P], ACT.Relu,
                                       bias=b2_sb[:, m:m + 1]).then_inc(h2_done, 1)

        @block.vector
        def _(dve):
            dve.memset(embT[:, :, :, :, NF:QUAD].rearrange("p t g s f -> p (t g s) f"), 0.0).then_inc(pad_done, 1)
            dve.memset(feats[:, :, FEATURES:K1 * P], 0.0).then_inc(pad_done, 1)
            dve.wait_ge(setup, SETUP)
            for n, chunks in enumerate(sorted(set(CHUNKS))):
                dve.tensor_copy(number[:, n, 0:chunks], number_i[:, n, 0:chunks]).then_inc(number_done, 1)

            def split_lo(k):
                n, r = CHUNKS[k], k % TABLE_RING
                dve.wait_ge(hi_done, k + 1)
                dve.tensor_tensor(lo[:, r, 0:n * DIM], raw[:, r, 0:n * DIM],
                                  hi[:, r, 0:n * DIM], ALU.subtract).then_inc(lo_done, 1)

            def select(k):
                size = sorted(set(CHUNKS)).index(CHUNKS[k])
                dve.wait_ge(ids_all_in[k % IDS_RING], 16 * (k // IDS_RING + 1))
                for c in range(CHUNKS[k]):
                    n = FIRST_CHUNK[k] + c
                    if n >= ONEHOT_RING:
                        dve.wait_ge(chunk_used, n - ONEHOT_RING + 1)
                    dve.tensor_scalar(onehot[:, n % ONEHOT_RING, :], ids_all[:, k % IDS_RING, :],
                                      number[:, size, c:c + 1], None, ALU.is_equal).then_inc(onehot_done, 1)

            dve.wait_ge(number_done, len(set(CHUNKS)))
            split_lo(0)
            for step in SCHEDULE:
                if step[0] == "select":
                    select(step[1])
                    if step[1] + 1 < NS:
                        split_lo(step[1] + 1)
                elif step[0] == "gram" and step[2] == STEPS - 1:
                    t = step[1]
                    dve.wait_ge(blocks_done, SIDE * STEPS * (t + 1))
                    if t:
                        dve.wait_ge(packed, len(COPIES) * t)
                    dve.transpose(square[:, 0:NF * QUAD].rearrange("p (j i) -> p j i", i=QUAD),
                                  blocks[:, :, :].rearrange("p g j -> p j g")).then_inc(square_done, 1)
                    dve.wait_ge(square_done, t + 1)
                    if t >= 2:
                        dve.wait_ge(featsT_full, t - 1)
                    at = 0
                    for first, pitch, count, width in COPIES:
                        src = square[:, first:first + pitch * count].rearrange("p (r x) -> p r x", x=pitch)
                        dst = feats[:, t % 2, at:at + count * width].rearrange("p (r x) -> p r x", x=width)
                        dve.tensor_copy(dst, src[:, :, 0:width]).then_inc(packed, 1)
                        at += count * width
                elif step[0] == "features":
                    t = step[1]
                    dve.wait_ge(featsT_full, t + 1)
                    if t:
                        dve.wait_ge(l1_full, t)
                    dve.tensor_copy(featsT[:, :], mlp_a[:, 0:K1 * P]).then_inc(featsT_done, 1)
                elif step[0] == "layer3":
                    t = step[1]
                    dve.wait_ge(l3_full, t + 1)
                    dve.tensor_copy(y_sb[:, t * P:(t + 1) * P], mlp_b[0:1, 0:P]).then_inc(y_done, 1)

        @block.tensor
        def _(pe):
            pe.wait_ge(setup, SETUP)
            for step in SCHEDULE:
                kind, t = step[0], step[1]
                if step in FEED:
                    n = FEED[step]
                    if n >= FEED_RING:
                        pe.wait_ge(feed_read, n - FEED_RING + 1)
                    bank = feed[:, n % FEED_RING, :]
                if kind == "select":
                    k = t
                    r = k % TABLE_RING
                    pe.wait_ge(hi_done, k + 1)
                    pe.wait_ge(lo_done, k + 1)
                    for c in range(CHUNKS[k]):
                        q = FIRST_CHUNK[k] + c
                        pe.wait_ge(onehot_done, q + 1)
                        for part, table in enumerate((hi, lo)):
                            last = pe.matmul(bank, table[:, r, c * DIM:(c + 1) * DIM], onehot[:, q % ONEHOT_RING, :],
                                             start=(c == 0 and part == 0), stop=(c == CHUNKS[k] - 1 and part == 1))
                        last.then_inc(chunk_used, 1)
                elif kind == "transpose":
                    g = step[2]
                    pe.wait_ge(gathered[t][g], 16 * len(LOOKUP_GROUPS[g]))
                    for x, m in enumerate(LOOKUP_GROUPS[g]):
                        last = pe.transpose(bank[:, x * P:(x + 1) * P], rows_sb[:, t, m, :], identity[:, :])
                    last.then_inc(transposed, 1)
                elif kind == "gram":
                    c = step[2]
                    n = t * STEPS + c
                    if c == 0:
                        pe.wait_ge(pad_done, 2)
                        pe.wait_ge(feed_read, 1 + max(m for s, m in FEED.items() if s[0] == "select" or s[1] == t))
                    if n >= 2:
                        pe.wait_ge(blocks_done, SIDE * (n - 1))
                    for g in range(STEP_GROUPS):
                        first = c * STEP_GROUPS + g
                        padded = embT[:, t, first, :, :].rearrange("p s f -> p (s f)")
                        four = embT[:, t, first, :, 0:NF]
                        last = pe.matmul(gram[:, n % 2, g // 4, (g % 4) * SIDE * NF:(g % 4 + 1) * SIDE * NF],
                                         padded, four, start=True, stop=True)
                    last.then_inc(gram_full, 1)
                elif kind == "features":
                    pe.wait_ge(dense_in[t % 2], 16 * (t // 2 + 1))
                    pe.wait_ge(packed, len(COPIES) * (t + 1))
                    if t:
                        pe.wait_ge(h2_done, K3 * t)
                    for k in range(K1):
                        last = pe.transpose(mlp_a[:, k * P:(k + 1) * P], feats[:, t % 2, k * P:(k + 1) * P], identity[:, :])
                    last.then_inc(featsT_full, 1)
                elif kind == "layer1":
                    pe.wait_ge(w_in, 16 * 5)
                    pe.wait_ge(featsT_done, t + 1)
                    if t:
                        pe.wait_ge(y_done, t)
                    for m in range(K2):
                        for k in range(K1):
                            last = pe.matmul(mlp_b[:, m * P:(m + 1) * P], w1_sb[:, k, m * P:(m + 1) * P],
                                             featsT[:, k * P:(k + 1) * P], start=(k == 0), stop=(k == K1 - 1))
                    last.then_inc(l1_full, 1)
                elif kind == "layer2":
                    pe.wait_ge(h1_done, K2 * (t + 1))
                    for m in range(K3):
                        for k in range(K2):
                            last = pe.matmul(mlp_a[:, m * P:(m + 1) * P], w2_sb[:, k, m * P:(m + 1) * P],
                                             h1T[:, k * P:(k + 1) * P], start=(k == 0), stop=(k == K2 - 1))
                    last.then_inc(l2_full, 1)
                elif kind == "layer3":
                    pe.wait_ge(h2_done, K3 * (t + 1))
                    for k in range(K3):
                        last = pe.matmul(mlp_b[0:1, 0:P], w3_sb[:, k:k + 1], h2T[:, k * P:(k + 1) * P],
                                         start=(k == 0), stop=(k == K3 - 1))
                    last.then_inc(l3_full, 1)


def kernel(**inputs):
    import concourse.bacc as bacc
    from concourse.bass_utils import run_bass_kernel_spmd

    def columns(v):
        return np.ascontiguousarray(np.asarray(v).reshape(-1, P).T)

    w1 = np.asarray(inputs["W_top1"])
    w1_rows = np.zeros((K1 * P, H1), w1.dtype)
    w1_rows[:FEATURES] = w1[feature_rows()]
    ids = np.ascontiguousarray(inputs["ids"])
    arrays = {
        "in_dense": np.ascontiguousarray(inputs["dense_ctx"]),
        "in_ids": ids,
        "in_ids_rows": np.ascontiguousarray(ids.T),
        **{f"in_tbl_{f}": np.ascontiguousarray(inputs[f"tbl_{f}"]) for f in range(NF)},
        "in_w1": w1_rows,
        "in_b1": columns(inputs["b_top1"]),
        "in_w2": np.ascontiguousarray(inputs["W_top2"]),
        "in_b2": columns(inputs["b_top2"]),
        "in_w3": columns(inputs["W_top3"]),
    }
    nc = bacc.Bacc("TRN2", target_bir_lowering=False, num_devices=1)
    dram = {name: nc.dram_tensor(name, a.shape, mybir.dt.from_np(a.dtype), kind="ExternalInput").ap()
            for name, a in arrays.items()}
    y = nc.dram_tensor("out_y", (BATCH, 1), FP32, kind="ExternalOutput").ap()
    tower(nc, dram["in_dense"], dram["in_ids"], dram["in_ids_rows"], [dram[f"in_tbl_{f}"] for f in range(NF)],
          dram["in_w1"], dram["in_b1"], dram["in_w2"], dram["in_b2"], dram["in_w3"], y)
    return run_bass_kernel_spmd(nc, [arrays], core_ids=[0]).results[0]["out_y"]
```

```python
from contextlib import ExitStack

import concourse.bass as bass
import concourse.mybir as mybir
import numpy as np

FP32 = mybir.dt.float32
FP32R = mybir.dt.float32r
INT32 = mybir.dt.int32
ALU = mybir.AluOpType
ACT = mybir.ActivationFunctionType

P = 128
BATCH = 512
DIM = 128
ROWS = [1250, 1000, 12500, 1250, 125000, 1000, 12500, 1000, 1000, 1250, 1000, 12500, 12500, 12500,
        12500, 1250, 1000, 1000, 1250, 12500, 12500, 1250, 1250, 1250, 1250, 1000, 1250]
NF = len(ROWS)
DENSE = 16
H1, H2 = 512, 256
TILES = BATCH // P

CHUNK = 125
SELECTED = sorted(sorted(range(NF), key=lambda f: (ROWS[f], f))[:9], key=lambda f: (ROWS[f], f))
LOOKED_UP = [f for f in range(NF) if f not in SELECTED]
SLOTS = LOOKED_UP + SELECTED
NS, NL = len(SELECTED), len(LOOKED_UP)
CHUNKS = [ROWS[f] // CHUNK for f in SELECTED]
MAX_CHUNKS = max(CHUNKS)
FIRST_CHUNK = [sum(CHUNKS[:k]) for k in range(NS + 1)]
FIRST_ONEHOT = [FIRST_CHUNK[k] - k for k in range(NS + 1)]
CHUNK_OF = [FIRST_CHUNK[k] + c for k in range(NS) for c in range(CHUNKS[k] - 1)]
SIZES = sorted(set(CHUNKS))
PER_BANK = 4
LOOKUP_GROUPS = [list(range(g, min(g + PER_BANK, NL))) for g in range(0, NL, PER_BANK)]
NG = len(LOOKUP_GROUPS)

QUAD = 32
SIDE = P // QUAD
USED = (SIDE - 1) * QUAD + NF
GROUPS = P // SIDE
STEP_GROUPS = 8
STEPS = GROUPS // STEP_GROUPS

WIDTH = 4


def pack_plan():
    copies, pairs = [], []
    blocks = range(1, NF, WIDTH)
    for b0 in blocks:
        rows = min(WIDTH, NF - b0)
        copies.append((b0 * QUAD, QUAD, rows, b0))
        pairs += [(a, b) for b in range(b0, b0 + rows) for a in range(b0)]
    for r in range(1, WIDTH):
        inner = [b0 for b0 in blocks if b0 + r < NF]
        copies.append(((1 + r) * QUAD + 1, WIDTH * (QUAD + 1), len(inner), r))
        pairs += [(b0 + x, b0 + r) for b0 in inner for x in range(r)]
    return copies, pairs


COPIES, PAIRS = pack_plan()
NPAIRS = NF * (NF - 1) // 2
FEATURES = NPAIRS + DENSE
K1 = -(-FEATURES // P)
K2, K3 = H1 // P, H2 // P
WRITTEN = [sum(count * width for _, _, count, width in COPIES[:n]) for n in range(len(COPIES) + 1)]
COPIES_OF = [min(n for n, w in enumerate(WRITTEN) if w >= min((k + 1) * P, NPAIRS)) for k in range(K1)]
ROOM = max(first + step * count for first, step, count, _ in COPIES)

WARM_UP = 10
KEEP_BUSY = 4
LATE = 1
SPREAD = [1, 1, 1, 2]
ONEHOT_RING = 10
RAW_RING = 3
TABLE_RING = 2
BY_SCALAR = 2
IDS_RING = 3


def feature_rows():
    at = []
    for a, b in PAIRS:
        i, j = sorted((SLOTS[a], SLOTS[b]))
        at.append(j * (j - 1) // 2 + i)
    return at + list(range(NPAIRS, FEATURES))


def schedule():
    lookups = [("transpose", t, g) for t in range(TILES) for g in range(NG)]
    order = []

    def add(*steps):
        for step in steps:
            if step[0] == "gram" and step[2] == 0:
                while lookups and lookups[0][1] <= step[1]:
                    order.append(lookups.pop(0))
            order.append(step)

    def add_lookups():
        order.append(lookups.pop(0))

    for k in range(NS):
        add(("select", k))
        if k >= LATE:
            add_lookups()
    for t in range(TILES):
        for c in range(STEPS):
            add(("gram", t, c))
            for _ in range(SPREAD[c]):
                if lookups and lookups[0][1] <= t + 1:
                    add_lookups()
            if t == TILES - 1:
                add(*[[("features", t - 1)], [("layer1", t - 1)], [], [("layer2", t - 1), ("layer3", t - 1)]][c])
            elif t:
                add(("features layer1 layer2 layer3".split()[c], t - 1))
    add(*[(stage, TILES - 1) for stage in ("features", "layer1", "layer2", "layer3")])
    return order


SCHEDULE = schedule()


def tower(nc, dense, ids, ids_rows, tables, w1, b1, w2, b2, w3, out):
    with ExitStack() as ctx:
        def sb(name, shape, dt=FP32):
            return ctx.enter_context(nc.sbuf_tensor(name, shape, dt))

        def ps(name, shape):
            return ctx.enter_context(nc.psum_tensor(name, shape, FP32))

        def sem(name):
            return ctx.enter_context(nc.semaphore(name))

        ids_sb = sb("ids_sb", [P, TILES, NF], INT32)
        rows_sb = sb("rows_sb", [P, TILES, NL, DIM])
        ids_all = sb("ids_all", [CHUNK, IDS_RING, BATCH], INT32)
        raw = sb("raw", [CHUNK, RAW_RING, MAX_CHUNKS * DIM])
        hi = sb("hi", [CHUNK, TABLE_RING, MAX_CHUNKS * DIM], FP32R)
        lo = sb("lo", [CHUNK, TABLE_RING, MAX_CHUNKS * DIM], FP32R)
        onehot = sb("onehot", [CHUNK, ONEHOT_RING, BATCH], FP32R)
        onehot_last = sb("onehot_last", [CHUNK, 2, BATCH], FP32R)
        distance = sb("distance", [CHUNK, BATCH])
        number_i = sb("number_i", [CHUNK, 2, MAX_CHUNKS], INT32)
        number = sb("number", [CHUNK, 2, MAX_CHUNKS])
        minus_last = sb("minus_last", [CHUNK, 2])
        embT = sb("embT", [P, TILES, GROUPS, SIDE, QUAD])
        identity = sb("identity", [P, P])
        blocks = sb("blocks", [P, GROUPS, NF])
        square = sb("square", [P, ROOM])
        feats = sb("feats", [P, 2, K1 * P])
        featsT = sb("featsT", [P, K1 * P])
        h1T = sb("h1T", [P, K2 * P])
        h2T = sb("h2T", [P, K3 * P])
        y_sb = sb("y_sb", [1, BATCH])
        w1_sb = sb("w1_sb", [P, K1, H1])
        w2_sb = sb("w2_sb", [P, K2, H2])
        w3_sb = sb("w3_sb", [P, K3])
        b1_sb = sb("b1_sb", [P, K2])
        b2_sb = sb("b2_sb", [P, K3])

        rowsT = ps("rowsT", [P, 2, BATCH])
        gram = ps("gram", [P, 2, 2, BATCH])
        mlp = ps("mlp", [P, 2, BATCH])

        ids_in = sem("ids_in")
        gathered = [[sem(f"gathered_{t}_{g}") for g in range(NG)] for t in range(TILES)]
        table_in = [sem(f"table_in_{r}") for r in range(RAW_RING)]
        ids_all_in = [sem(f"ids_all_in_{r}") for r in range(IDS_RING)]
        w_in = sem("w_in")
        dense_in = [sem(f"dense_in_{t}") for t in range(2)]
        out_done = sem("out_done")
        setup = sem("setup")
        number_done = sem("number_done")
        pad_done = sem("pad_done")
        hi_done = sem("hi_done")
        lo_done = sem("lo_done")
        negated = sem("negated")
        onehot_done = sem("onehot_done")
        distance_done = sem("distance_done")
        last_done = sem("last_done")
        chunk_used = sem("chunk_used")
        transposed = sem("transposed")
        lookups_read = sem("lookups_read")
        selected_read = sem("selected_read")
        gram_full = sem("gram_full")
        blocks_act = sem("blocks_act")
        blocks_dve = sem("blocks_dve")
        square_done = sem("square_done")
        packed = sem("packed")
        featsT_full = sem("featsT_full")
        featsT_done = sem("featsT_done")
        l1_full = sem("l1_full")
        h1_done = sem("h1_done")
        l2_full = sem("l2_full")
        h2_done = sem("h2_done")
        l3_full = sem("l3_full")
        y_done = sem("y_done")

        def block_in(n, q):
            rows = gram[q * QUAD:min((q + 1) * QUAD, USED), n % 2, :, 0:4 * SIDE * NF]
            return rows.rearrange("p b (g m) -> p b g m", g=4)[:, :, :, q * NF:(q + 1) * NF]

        def block_out(c, q):
            rows = blocks[q * QUAD:min((q + 1) * QUAD, USED), c * STEP_GROUPS:(c + 1) * STEP_GROUPS, :]
            return rows.rearrange("p (b g) f -> p b g f", b=2)

        block = ctx.enter_context(nc.Block())

        @block.sync
        def _(sp):
            def load_selected(k):
                f, n = SELECTED[k], CHUNKS[k]
                if k >= IDS_RING:
                    sp.wait_ge(onehot_done, FIRST_ONEHOT[k - IDS_RING + 1])
                    sp.wait_ge(distance_done, k - IDS_RING + 1)
                sp.dma_start(ids_all[:, k % IDS_RING, :],
                             ids_rows[f:f + 1, :].broadcast_to([CHUNK, BATCH])).then_inc(ids_all_in[k % IDS_RING], 16)
                if k < BY_SCALAR:
                    return
                if k >= RAW_RING:
                    sp.wait_ge(hi_done, k - RAW_RING + 1)
                    sp.wait_ge(lo_done, k - RAW_RING + 1)
                sp.dma_start(raw[:, k % RAW_RING, 0:n * DIM],
                             tables[f].rearrange("(p c) d -> p (c d)", c=n)).then_inc(table_in[k % RAW_RING], 16)

            sp.dma_start(ids_sb[:, :, :], ids).then_inc(ids_in, 16)
            load_selected(0)
            load_selected(1)
            load_selected(2)
            sp.dma_start(w1_sb[:, :, :], w1.rearrange("(k p) n -> p k n", p=P)).then_inc(w_in, 16)
            sp.dma_start(w2_sb[:, :, :], w2.rearrange("(k p) n -> p k n", p=P)).then_inc(w_in, 16)
            for dst, src in ((w3_sb, w3), (b1_sb, b1), (b2_sb, b2)):
                sp.dma_start(dst[:, :], src).then_inc(w_in, 16)

            def load_dense(t):
                if t >= 2:
                    sp.wait_ge(featsT_full, t - 1)
                sp.dma_start(feats[:, t % 2, NPAIRS:FEATURES], dense[t * P:(t + 1) * P, :]).then_inc(dense_in[t % 2], 16)

            load_dense(0)
            load_dense(1)
            for k in range(3, NS):
                load_selected(k)
            load_dense(2)
            load_dense(3)
            sp.wait_ge(y_done, TILES)
            sp.dma_start(out.rearrange("n o -> o n"), y_sb[:, :]).then_inc(out_done, 16)
            sp.wait_ge(out_done, 16)

        @block.gpsimd
        def _(pool):
            for n, chunks in enumerate(SIZES):
                pool.iota(number_i[:, n, 0:chunks], pattern=[[1, chunks]], base=0,
                          channel_multiplier=chunks).then_inc(setup, 1)
            pool.memset(identity[:, :], 0.0).then_inc(setup, 1)
            constants = len(SIZES) + 1
            pool.wait_ge(setup, constants)
            pool.affine_select(out=identity[:, :], in_=identity[:, :], compare_op=ALU.not_equal, fill=1.0,
                               base=0, pattern=[[-1, P]], channel_multiplier=1).then_inc(setup, 1)
            pool.wait_ge(ids_in, 16)
            for t in range(TILES):
                for g, group in enumerate(LOOKUP_GROUPS):
                    for n in group:
                        f = LOOKED_UP[n]
                        pool.indirect_dma_start(
                            rows_sb[:, t, n, :], None, tables[f],
                            bass.IndirectOffsetOnAxis(ap=ids_sb[:, t, f:f + 1], axis=0),
                        ).then_inc(gathered[t][g], 16)

        SETUP = len(SIZES) + 2

        @block.scalar
        def _(act):
            def split_hi(k):
                n, r = CHUNKS[k], k % TABLE_RING
                act.wait_ge(table_in[k % RAW_RING], 16 * (k // RAW_RING + 1))
                if k >= TABLE_RING:
                    act.wait_ge(chunk_used, FIRST_CHUNK[k - TABLE_RING + 1])
                act.activation(hi[:, r, 0:n * DIM], raw[:, k % RAW_RING, 0:n * DIM], ACT.Copy).then_inc(hi_done, 1)

            def read_selected(k):
                act.wait_ge(chunk_used, FIRST_CHUNK[k + 1])
                act.activation(embT[:, :, :, :, NL + k].rearrange("p t g s -> p t s g"),
                               mlp[:, k % 2, :].rearrange("p (t s g) -> p t s g", t=TILES, s=SIDE),
                               ACT.Copy).then_inc(selected_read, 1)

            def read_lookups(t, g):
                group = LOOKUP_GROUPS[g]
                act.wait_ge(transposed, t * NG + g + 1)
                act.activation(embT[:, t, :, :, group[0]:group[-1] + 1].rearrange("p g s f -> p f s g"),
                               rowsT[:, (t * NG + g) % 2, 0:len(group) * P].rearrange(
                                   "p (f s g) -> p f s g", s=SIDE, g=GROUPS),
                               ACT.Copy).then_inc(lookups_read, 1)

            for k in range(BY_SCALAR):
                f, n = SELECTED[k], CHUNKS[k]
                act.dma_start(raw[:, k, 0:n * DIM], tables[f].rearrange("(p c) d -> p (c d)", c=n)).then_inc(table_in[k], 16)

            def select_last(k):
                act.wait_ge(ids_all_in[k % IDS_RING], 16 * (k // IDS_RING + 1))
                size = SIZES.index(CHUNKS[k])
                if k:
                    act.wait_ge(last_done, k)
                act.activation(distance[:, :], ids_all[:, k % IDS_RING, :], ACT.Abs,
                               bias=minus_last[:, size:size + 1]).then_inc(distance_done, 1)
                act.wait_ge(distance_done, k + 1)
                if k >= 2:
                    act.wait_ge(chunk_used, FIRST_CHUNK[k - 1])
                act.activation(onehot_last[:, k % 2, :], distance[:, :], ACT.Relu,
                               bias=1.0, scale=-1.0).then_inc(last_done, 1)

            split_hi(0)
            split_hi(1)
            act.wait_ge(number_done, len(SIZES))
            for n, chunks in enumerate(SIZES):
                act.activation(minus_last[:, n:n + 1], number[:, n, chunks - 1:chunks], ACT.Copy,
                               scale=-1.0).then_inc(negated, 1)
            act.wait_ge(negated, len(SIZES))
            select_last(0)
            for step in SCHEDULE:
                if step[0] == "select":
                    if step[1] + 1 < NS:
                        select_last(step[1] + 1)
                    read_selected(step[1])
                    if step[1] + 2 < NS:
                        split_hi(step[1] + 2)
                elif step[0] == "transpose":
                    read_lookups(step[1], step[2])
                elif step[0] == "gram":
                    _, t, c = step
                    n = t * STEPS + c
                    act.wait_ge(gram_full, n + 1)
                    if t and c == 0:
                        act.wait_ge(square_done, t)
                    for q in range(SIDE // 2):
                        act.activation(block_out(c, q), block_in(n, q), ACT.Copy).then_inc(blocks_act, 1)
                elif step[0] == "layer1":
                    t = step[1]
                    act.wait_ge(w_in, 16 * 5)
                    if t:
                        act.wait_ge(l2_full, K3 * t)
                    for m in range(K2):
                        if m % 2 == 0:
                            act.wait_ge(l1_full, 2 * t + m // 2 + 1)
                        act.activation(h1T[:, m * P:(m + 1) * P], mlp[:, m // 2, (m % 2) * P:(m % 2 + 1) * P],
                                       ACT.Relu, bias=b1_sb[:, m:m + 1]).then_inc(h1_done, 1)
                elif step[0] == "layer2":
                    t = step[1]
                    if t:
                        act.wait_ge(l3_full, t)
                    for m in range(K3):
                        act.wait_ge(l2_full, K3 * t + m + 1)
                        act.activation(h2T[:, m * P:(m + 1) * P], mlp[:, m, 0:P], ACT.Relu,
                                       bias=b2_sb[:, m:m + 1]).then_inc(h2_done, 1)

        @block.vector
        def _(dve):
            dve.wait_ge(setup, SETUP)
            for n, chunks in enumerate(SIZES):
                dve.tensor_copy(number[:, n, 0:chunks], number_i[:, n, 0:chunks]).then_inc(number_done, 1)

            def split_lo(k):
                n, r = CHUNKS[k], k % TABLE_RING
                dve.wait_ge(hi_done, k + 1)
                dve.tensor_tensor(lo[:, r, 0:n * DIM], raw[:, k % RAW_RING, 0:n * DIM],
                                  hi[:, r, 0:n * DIM], ALU.subtract).then_inc(lo_done, 1)

            def select(k):
                size = SIZES.index(CHUNKS[k])
                dve.wait_ge(ids_all_in[k % IDS_RING], 16 * (k // IDS_RING + 1))
                for c in range(CHUNKS[k] - 1):
                    n = FIRST_ONEHOT[k] + c
                    if n >= ONEHOT_RING:
                        dve.wait_ge(chunk_used, CHUNK_OF[n - ONEHOT_RING] + 1)
                    dve.tensor_scalar(onehot[:, n % ONEHOT_RING, :], ids_all[:, k % IDS_RING, :],
                                      number[:, size, c:c + 1], None, ALU.is_equal).then_inc(onehot_done, 1)

            dve.wait_ge(number_done, len(SIZES))
            zeros = [embT[:, :, :, :, NF:QUAD].rearrange("p t g s f -> p (t g s) f"),
                     blocks[P - QUAD:P, :, :], feats[:, :, FEATURES:K1 * P]]
            for step in SCHEDULE:
                if step[0] == "select":
                    select(step[1])
                    if step[1] == 0:
                        split_lo(0)
                    if step[1] + 1 < NS:
                        split_lo(step[1] + 1)
                    else:
                        for part in zeros:
                            dve.memset(part, 0.0).then_inc(pad_done, 1)
                elif step[0] == "gram":
                    _, t, c = step
                    n = t * STEPS + c
                    if n == 0:
                        dve.wait_ge(pad_done, 3)
                    dve.wait_ge(gram_full, n + 1)
                    if t and c == 0:
                        dve.wait_ge(square_done, t)
                    for q in range(SIDE // 2, SIDE):
                        dve.tensor_copy(block_out(c, q), block_in(n, q)).then_inc(blocks_dve, 1)
                    if c < STEPS - 1:
                        continue
                    dve.wait_ge(blocks_act, 2 * STEPS * (t + 1))
                    dve.wait_ge(blocks_dve, 2 * STEPS * (t + 1))
                    if t:
                        dve.wait_ge(packed, len(COPIES) * t)
                    dve.transpose(square[:, 0:NF * QUAD].rearrange("p (j i) -> p j i", i=QUAD),
                                  blocks[:, :, :].rearrange("p g j -> p j g")).then_inc(square_done, 1)
                    dve.wait_ge(square_done, t + 1)
                    if t >= 2:
                        dve.wait_ge(featsT_full, t - 1)
                    at = 0
                    for first, pitch, count, width in COPIES:
                        src = square[:, first:first + pitch * count].rearrange("p (r x) -> p r x", x=pitch)
                        dst = feats[:, t % 2, at:at + count * width].rearrange("p (r x) -> p r x", x=width)
                        dve.tensor_copy(dst, src[:, :, 0:width]).then_inc(packed, 1)
                        at += count * width
                elif step[0] == "features":
                    t = step[1]
                    dve.wait_ge(featsT_full, t + 1)
                    if t:
                        dve.wait_ge(l1_full, 2 * t)
                    dve.tensor_copy(featsT[:, :], mlp[:, 0, 0:K1 * P]).then_inc(featsT_done, 1)
                elif step[0] == "layer3":
                    t = step[1]
                    dve.wait_ge(l3_full, t + 1)
                    dve.tensor_copy(y_sb[:, t * P:(t + 1) * P], mlp[0:1, 0, 0:P]).then_inc(y_done, 1)

        @block.tensor
        def _(pe):
            pe.wait_ge(setup, SETUP)

            def keep_busy(times):
                for _ in range(times):
                    pe.matmul(mlp[:, 1, 0:P], identity[:, :], identity[:, :], start=True, stop=True)

            keep_busy(WARM_UP)
            for step in SCHEDULE:
                kind, t = step[0], step[1]
                if kind == "select":
                    k = t
                    r = k % TABLE_RING
                    n = CHUNKS[k]
                    bank = mlp[:, k % 2, :]
                    if k >= 2:
                        pe.wait_ge(selected_read, k - 1)
                    pe.wait_ge(hi_done, k + 1)

                    def moving(c):
                        if c == n - 1:
                            pe.wait_ge(last_done, k + 1)
                            return onehot_last[:, k % 2, :]
                        q = FIRST_ONEHOT[k] + c
                        pe.wait_ge(onehot_done, q + 1)
                        return onehot[:, q % ONEHOT_RING, :]

                    if k == 0:
                        for c in range(n):
                            pe.matmul(bank, hi[:, r, c * DIM:(c + 1) * DIM], moving(c), start=(c == 0), stop=False)
                        pe.wait_ge(lo_done, 1)
                        for c in range(n):
                            pe.matmul(bank, lo[:, r, c * DIM:(c + 1) * DIM], moving(c), start=False,
                                      stop=(c == n - 1)).then_inc(chunk_used, 1)
                        continue
                    pe.wait_ge(lo_done, k + 1)
                    for c in range(n):
                        ones = moving(c)
                        pe.matmul(bank, hi[:, r, c * DIM:(c + 1) * DIM], ones, start=(c == 0), stop=False)
                        pe.matmul(bank, lo[:, r, c * DIM:(c + 1) * DIM], ones, start=False,
                                  stop=(c == n - 1)).then_inc(chunk_used, 1)
                elif kind == "transpose":
                    g = step[2]
                    pe.wait_ge(gathered[t][g], 16 * len(LOOKUP_GROUPS[g]))
                    n = t * NG + g
                    if n >= 2:
                        pe.wait_ge(lookups_read, n - 1)
                    for x, m in enumerate(LOOKUP_GROUPS[g]):
                        last = pe.transpose(rowsT[:, n % 2, x * P:(x + 1) * P], rows_sb[:, t, m, :], identity[:, :])
                    last.then_inc(transposed, 1)
                elif kind == "gram":
                    c = step[2]
                    n = t * STEPS + c
                    if c == 0:
                        pe.wait_ge(pad_done, 3)
                        pe.wait_ge(selected_read, NS)
                        pe.wait_ge(lookups_read, NG * (t + 1))
                    if n >= 2:
                        pe.wait_ge(blocks_act, 2 * (n - 1))
                        pe.wait_ge(blocks_dve, 2 * (n - 1))
                    for g in range(STEP_GROUPS):
                        first = c * STEP_GROUPS + g
                        padded = embT[:, t, first, :, :].rearrange("p s f -> p (s f)")[:, 0:USED]
                        four = embT[:, t, first, :, 0:NF]
                        last = pe.matmul(gram[0:USED, n % 2, g // 4, (g % 4) * SIDE * NF:(g % 4 + 1) * SIDE * NF],
                                         padded, four, start=True, stop=True)
                    last.then_inc(gram_full, 1)
                elif kind == "features":
                    if t:
                        pe.wait_ge(y_done, t)
                    for k in range(K1):
                        if k == K1 - 1:
                            pe.wait_ge(dense_in[t % 2], 16 * (t // 2 + 1))
                        pe.wait_ge(packed, len(COPIES) * t + COPIES_OF[k])
                        last = pe.transpose(mlp[:, 0, k * P:(k + 1) * P], feats[:, t % 2, k * P:(k + 1) * P], identity[:, :])
                    last.then_inc(featsT_full, 1)
                    if t == TILES - 1:
                        keep_busy(KEEP_BUSY)
                elif kind == "layer1":
                    pe.wait_ge(w_in, 16 * 5)
                    pe.wait_ge(featsT_done, t + 1)
                    for m in range(K2):
                        for k in range(K1):
                            last = pe.matmul(mlp[:, m // 2, (m % 2) * P:(m % 2 + 1) * P], w1_sb[:, k, m * P:(m + 1) * P],
                                             featsT[:, k * P:(k + 1) * P], start=(k == 0), stop=(k == K1 - 1))
                        if m % 2:
                            last.then_inc(l1_full, 1)
                elif kind == "layer2":
                    for m in range(K3):
                        for k in range(K2):
                            pe.wait_ge(h1_done, K2 * t + max(k + 1, 2))
                            last = pe.matmul(mlp[:, m, 0:P], w2_sb[:, k, m * P:(m + 1) * P],
                                             h1T[:, k * P:(k + 1) * P], start=(k == 0), stop=(k == K2 - 1))
                        last.then_inc(l2_full, 1)
                elif kind == "layer3":
                    for k in range(K3):
                        pe.wait_ge(h2_done, K3 * t + k + 1)
                        last = pe.matmul(mlp[0:1, 0, 0:P], w3_sb[:, k:k + 1], h2T[:, k * P:(k + 1) * P],
                                         start=(k == 0), stop=(k == K3 - 1))
                    last.then_inc(l3_full, 1)


def kernel(**inputs):
    import concourse.bacc as bacc
    from concourse.bass_utils import run_bass_kernel_spmd

    def columns(v):
        return np.ascontiguousarray(np.asarray(v).reshape(-1, P).T)

    w1 = np.asarray(inputs["W_top1"])
    w1_rows = np.zeros((K1 * P, H1), w1.dtype)
    w1_rows[:FEATURES] = w1[feature_rows()]
    ids = np.ascontiguousarray(inputs["ids"])
    arrays = {
        "in_dense": np.ascontiguousarray(inputs["dense_ctx"]),
        "in_ids": np.ascontiguousarray(ids.reshape(TILES, P, NF).transpose(1, 0, 2)),
        "in_ids_rows": np.ascontiguousarray(ids.T),
        **{f"in_tbl_{f}": np.ascontiguousarray(inputs[f"tbl_{f}"]) for f in range(NF)},
        "in_w1": w1_rows,
        "in_b1": columns(inputs["b_top1"]),
        "in_w2": np.ascontiguousarray(inputs["W_top2"]),
        "in_b2": columns(inputs["b_top2"]),
        "in_w3": columns(inputs["W_top3"]),
    }
    nc = bacc.Bacc("TRN2", target_bir_lowering=False, num_devices=1)
    dram = {name: nc.dram_tensor(name, a.shape, mybir.dt.from_np(a.dtype), kind="ExternalInput").ap()
            for name, a in arrays.items()}
    y = nc.dram_tensor("out_y", (BATCH, 1), FP32, kind="ExternalOutput").ap()
    tower(nc, dram["in_dense"], dram["in_ids"], dram["in_ids_rows"], [dram[f"in_tbl_{f}"] for f in range(NF)],
          dram["in_w1"], dram["in_b1"], dram["in_w2"], dram["in_b2"], dram["in_w3"], y)
    return run_bass_kernel_spmd(nc, [arrays], core_ids=[0]).results[0]["out_y"]
```

```python
from contextlib import ExitStack

import concourse.bass as bass
import concourse.mybir as mybir
import numpy as np

FP32 = mybir.dt.float32
FP32R = mybir.dt.float32r
INT32 = mybir.dt.int32
ALU = mybir.AluOpType
ACT = mybir.ActivationFunctionType

P = 128
BATCH = 512
DIM = 128
ROWS = [1250, 1000, 12500, 1250, 125000, 1000, 12500, 1000, 1000, 1250, 1000, 12500, 12500, 12500,
        12500, 1250, 1000, 1000, 1250, 12500, 12500, 1250, 1250, 1250, 1250, 1000, 1250]
NF = len(ROWS)
DENSE = 16
H1, H2 = 512, 256
TILES = BATCH // P

CHUNK = 125
SELECTED = sorted(sorted(range(NF), key=lambda f: (ROWS[f], f))[:9], key=lambda f: (ROWS[f], f))
LOOKED_UP = [f for f in range(NF) if f not in SELECTED]
SLOTS = LOOKED_UP + SELECTED
NS, NL = len(SELECTED), len(LOOKED_UP)
CHUNKS = [ROWS[f] // CHUNK for f in SELECTED]
MAX_CHUNKS = max(CHUNKS)
FIRST_CHUNK = [sum(CHUNKS[:k]) for k in range(NS + 1)]
BY_ACT = [1] * NS
FIRST_ACT = [sum(BY_ACT[:k]) for k in range(NS + 1)]
FIRST_DVE = [FIRST_CHUNK[k] - FIRST_ACT[k] for k in range(NS + 1)]
ACT_CHUNKS = [FIRST_CHUNK[k + 1] - BY_ACT[k] + c for k in range(NS) for c in range(BY_ACT[k])]
DVE_CHUNKS = [FIRST_CHUNK[k] + c for k in range(NS) for c in range(CHUNKS[k] - BY_ACT[k])]
SIZES = sorted(set(CHUNKS))
PER_BANK = 4
LOOKUP_GROUPS = [list(range(g, min(g + PER_BANK, NL))) for g in range(0, NL, PER_BANK)]
NG = len(LOOKUP_GROUPS)

QUAD = 32
SIDE = P // QUAD
GROUPS = P // SIDE
WHOLE, SPLIT = [0, 3], [1, 2]
COLUMN_TILES = WHOLE + SPLIT
SPLIT_COLUMNS = len(WHOLE) * P
STEP_GROUPS = [8 if t in WHOLE else 4 for t in range(TILES)]
STEPS = [GROUPS // n for n in STEP_GROUPS]
FIRST_STEP = [sum(STEPS[:t]) for t in range(TILES + 1)]

WIDTH = 4


def pack_plan():
    steps, pairs = [], []
    blocks = range(1, NF, WIDTH)
    for b0 in blocks:
        rows = min(WIDTH, NF - b0)
        steps.append(("rectangle", b0, rows, b0))
        pairs += [(a, b) for b in range(b0, b0 + rows) for a in range(b0)]
    for r in range(1, WIDTH):
        inner = [b0 for b0 in blocks if b0 + r < NF]
        steps.append(("triangles", r, len(inner), r))
        pairs += [(b0 + x, b0 + r) for b0 in inner for x in range(r)]
    return steps, pairs


def pair_views(square, kind, at, count, width):
    if kind == "rectangle":
        ba = square[:, at * QUAD:(at + count) * QUAD].rearrange("p (r x) -> p r x", x=QUAD)
        ab = square[:, 0:width * QUAD].rearrange("p (x r) -> p r x", r=QUAD)
        return ba[:, :, 0:width], ab[:, at:at + count, :]
    diagonal = WIDTH * (QUAD + 1)
    first = (1 + at) * QUAD + 1
    ba = square[:, first:first + diagonal * count].rearrange("p (i y) -> p i y", y=diagonal)
    first = QUAD + 1 + at
    ab = square[:, first:first + diagonal * count].rearrange("p (i y) -> p i y", y=diagonal)
    ab = ab[:, :, 0:WIDTH * QUAD].rearrange("p i (x y) -> p i x y", y=QUAD)
    return ba[:, :, 0:width], ab[:, :, 0:width, 0]


PACKING, PAIRS = pack_plan()
NPAIRS = NF * (NF - 1) // 2
FEATURES = NPAIRS + DENSE
K1 = -(-FEATURES // P)
K2, K3 = H1 // P, H2 // P
WRITTEN = [sum(count * width for *_, count, width in PACKING[:n]) for n in range(len(PACKING) + 1)]
PACKED_BY = [min(n for n, w in enumerate(WRITTEN) if w >= min((k + 1) * P, NPAIRS)) for k in range(K1)]
ROOM = WIDTH * (QUAD + 1) * -(-NF // WIDTH) + 2 * QUAD + 1

ONEHOT_RING = 14
ACT_RING = 3
RAW_RING = 3
TABLE_RING = 2
IDS_RING = 3
ROWS_RING = 8

WARM_UP = 10
LOADED_BY_ACT = 2
PAD_FROM = 3
ACT_QUADS = 2
SELECT_LOOKUPS = [0, 0, 1, 1, 1, 0, 1, 2, 1]
AFTER = [["L", "L", "L", "LP"],
         ["", "L", "F", "aL", "b", "L", "c", "LdlP"],
         ["z", "", "LF", "aL", "b", "L", "cL", "dlPL"],
         ["z", "F", "a", "bPcd"]]
END = "Fzabcdy"
STAGES = {"F": ("features", 0, 1), "a": ("layer1", 0, 1), "b": ("layer1", 1, 1), "c": ("layer2", 0, 1),
          "d": ("layer2", 1, 1), "y": ("layer3", 0, 1), "z": ("layer3", 0, 2)}


def feature_rows():
    at = []
    for a, b in PAIRS:
        i, j = sorted((SLOTS[a], SLOTS[b]))
        at.append(j * (j - 1) // 2 + i)
    return at + list(range(NPAIRS, FEATURES))


def low_groups(n):
    return sum(group // NG in SPLIT for group in range(n))


def schedule():
    lookups = [(t, g) for t in range(TILES) for g in range(NG)]
    high_only = []
    order = []

    def transpose():
        order.append(("transpose", *lookups[0]))
        if lookups[0][0] in SPLIT:
            high_only.append(lookups[0])
        lookups.pop(0)

    def low_parts(leave=0):
        while len(high_only) > leave:
            order.append(("low", *high_only.pop(0)))

    for k in range(NS):
        order.append(("select", k))
        low_parts()
        for _ in range(SELECT_LOOKUPS[k]):
            transpose()

    def follow(plan, t):
        for letter in plan:
            if letter == "L":
                low_parts(1)
                transpose()
            elif letter == "l":
                low_parts()
            elif letter == "P":
                order.append(("pack", t))
            else:
                stage, part, back = STAGES[letter]
                order.append((stage, t - back, part))

    for t in range(TILES):
        while lookups and lookups[0][0] <= t:
            low_parts(1)
            transpose()
        low_parts()
        for c in range(STEPS[t]):
            order.append(("gram", t, c))
            low_parts()
            follow(AFTER[t][c], t)
    follow(END, TILES)
    return order


SCHEDULE = schedule()


def tower(nc, dense, ids, ids_rows, tables, w1, b1, w2, b2, w3, out):
    with ExitStack() as ctx:
        def sb(name, shape, dt=FP32):
            return ctx.enter_context(nc.sbuf_tensor(name, shape, dt))

        selecting = ExitStack()

        def sel(name, shape, dt=FP32):
            return selecting.enter_context(nc.sbuf_tensor(name, shape, dt))

        def ps(name, shape):
            return ctx.enter_context(nc.psum_tensor(name, shape, FP32))

        def sem(name):
            return ctx.enter_context(nc.semaphore(name))

        ids_sb = sb("ids_sb", [P, TILES, NF], INT32)
        rows_sb = sb("rows_sb", [P, ROWS_RING, PER_BANK, DIM])
        wholeT = sb("wholeT", [P, len(WHOLE), GROUPS, SIDE, QUAD])
        splitT = sb("splitT", [P, len(SPLIT), GROUPS, 2, SIDE, QUAD], FP32R)
        identity = sb("identity", [P, P])
        zero = sb("zero", [P, 1])
        feats = sb("feats", [P, 2, K1 * P])
        w3_sb = sb("w3_sb", [P, K3])
        b1_sb = sb("b1_sb", [P, K2])
        b2_sb = sb("b2_sb", [P, K3])
        ids_all = sel("ids_all", [CHUNK, IDS_RING, BATCH], INT32)
        raw = sel("raw", [CHUNK, RAW_RING, MAX_CHUNKS * DIM])
        hi = sel("hi", [CHUNK, TABLE_RING, MAX_CHUNKS * DIM], FP32R)
        lo = sel("lo", [CHUNK, TABLE_RING, MAX_CHUNKS * DIM], FP32R)
        onehot = sel("onehot", [CHUNK, ONEHOT_RING, BATCH], FP32R)
        onehot_act = sel("onehot_act", [CHUNK, ACT_RING, BATCH], FP32R)
        number_i = sel("number_i", [CHUNK, 2, MAX_CHUNKS], INT32)
        number = sel("number", [CHUNK, 2, MAX_CHUNKS])
        minus = sel("minus", [CHUNK, 2, MAX_CHUNKS])
        selecting.close()
        w1_sb = sb("w1_sb", [P, K1, H1])
        w2_sb = sb("w2_sb", [P, K2, H2])
        blocks = sb("blocks", [P, GROUPS, 2, NF])
        sums = sb("sums", [P, 2, GROUPS, NF])
        square = sb("square", [P, ROOM])
        featsT = sb("featsT", [P, K1 * P])
        h1T = sb("h1T", [P, K2 * P])
        h2T = sb("h2T", [P, K3 * P])
        y_sb = sb("y_sb", [1, BATCH])

        rowsT = ps("rowsT", [P, 2, BATCH])
        gram = ps("gram", [P, 2, 2, BATCH])
        mlp = ps("mlp", [P, 2, BATCH])

        ids_in = sem("ids_in")
        gathered = [[sem(f"gathered_{t}_{g}") for g in range(NG)] for t in range(TILES)]
        table_in = [sem(f"table_in_{r}") for r in range(RAW_RING)]
        ids_all_in = [sem(f"ids_all_in_{r}") for r in range(IDS_RING)]
        w_in = sem("w_in")
        dense_in = [sem(f"dense_in_{t}") for t in range(2)]
        out_done = sem("out_done")
        setup = sem("setup")
        number_done = sem("number_done")
        negated = sem("negated")
        pad_done = sem("pad_done")
        low_padded = sem("low_padded")
        hi_done = sem("hi_done")
        lo_done = sem("lo_done")
        onehot_done = sem("onehot_done")
        distance_done = sem("distance_done")
        onehot_act_done = sem("onehot_act_done")
        chunk_used = sem("chunk_used")
        transposed = sem("transposed")
        lookups_read = sem("lookups_read")
        selected_read = sem("selected_read")
        last_read = sem("last_read")
        gram_full = sem("gram_full")
        blocks_act = sem("blocks_act")
        blocks_dve = sem("blocks_dve")
        lookups_low = sem("lookups_low")
        summed = sem("summed")
        square_done = sem("square_done")
        packed = sem("packed")
        featsT_full = sem("featsT_full")
        featsT_done = sem("featsT_done")
        l1_full = sem("l1_full")
        h1_done = sem("h1_done")
        l2_full = sem("l2_full")
        h2_done = sem("h2_done")
        l3_full = sem("l3_full")
        y_done = sem("y_done")

        def features_bank(t):
            return mlp[:, 0, :] if t < TILES - 1 else rowsT[:, 0, :]

        def layer_bank(t, n):
            return mlp[:, n, :] if t < TILES - 1 else gram[:, 0, n, :]

        def block_in(t, n, q):
            rows = gram[q * QUAD:(q + 1) * QUAD, n % 2, :, :]
            if t in WHOLE:
                rows = rows[:, :, 0:4 * SIDE * NF].rearrange("p b (g m) -> p b g m", g=4)
                return rows[:, :, :, q * NF:(q + 1) * NF]
            return rows.rearrange("p b (g m x) -> p (b g) m x", m=2, x=P)[:, :, :, q * QUAD:q * QUAD + NF]

        def block_out(t, c, q):
            groups = slice(c * STEP_GROUPS[t], (c + 1) * STEP_GROUPS[t])
            if t in WHOLE:
                return sums[q * QUAD:(q + 1) * QUAD, t % 2, groups, :].rearrange("p (b g) f -> p b g f", b=2)
            return blocks[q * QUAD:(q + 1) * QUAD, groups, :, :]

        block = ctx.enter_context(nc.Block())

        @block.sync
        def _(sp):
            def load_selected(k):
                f, n = SELECTED[k], CHUNKS[k]
                if k >= IDS_RING:
                    sp.wait_ge(onehot_done, FIRST_DVE[k - IDS_RING + 1])
                    sp.wait_ge(distance_done, FIRST_ACT[k - IDS_RING + 1])
                sp.dma_start(ids_all[:, k % IDS_RING, :],
                             ids_rows[f:f + 1, :].broadcast_to([CHUNK, BATCH])
                             ).then_inc(ids_all_in[k % IDS_RING], 16)
                if k < LOADED_BY_ACT:
                    return
                if k >= RAW_RING:
                    sp.wait_ge(hi_done, 2 * (k - RAW_RING + 1))
                    sp.wait_ge(lo_done, 2 * (k - RAW_RING + 1))
                sp.dma_start(raw[:, k % RAW_RING, 0:n * DIM],
                             tables[f].rearrange("(p c) d -> p (c d)", c=n)).then_inc(table_in[k % RAW_RING], 16)

            sp.dma_start(ids_sb[:, :, :], ids).then_inc(ids_in, 16)
            load_selected(0)
            load_selected(1)
            for dst, src in ((w3_sb, w3), (b1_sb, b1), (b2_sb, b2)):
                sp.dma_start(dst[:, :], src).then_inc(w_in, 16)

            def load_dense(t):
                if t >= 2:
                    sp.wait_ge(featsT_full, t - 1)
                sp.dma_start(feats[:, t % 2, NPAIRS:FEATURES],
                             dense[t * P:(t + 1) * P, :]).then_inc(dense_in[t % 2], 16)

            load_dense(0)
            load_dense(1)
            for k in range(2, NS):
                load_selected(k)
            sp.wait_ge(chunk_used, FIRST_CHUNK[NS])
            sp.dma_start(w1_sb[:, :, :], w1.rearrange("(k p) n -> p k n", p=P)).then_inc(w_in, 16)
            sp.dma_start(w2_sb[:, :, :], w2.rearrange("(k p) n -> p k n", p=P)).then_inc(w_in, 16)
            load_dense(2)
            load_dense(3)
            sp.wait_ge(y_done, TILES)
            sp.dma_start(out.rearrange("n o -> o n"), y_sb[:, :]).then_inc(out_done, 16)
            sp.wait_ge(out_done, 16)

        @block.gpsimd
        def _(pool):
            for n, chunks in enumerate(SIZES):
                pool.iota(number_i[:, n, 0:chunks], pattern=[[1, chunks]], base=0,
                          channel_multiplier=chunks).then_inc(setup, 1)
            pool.memset(identity[:, :], 0.0).then_inc(setup, 1)
            pool.memset(zero[:, :], 0.0).then_inc(setup, 1)
            constants = len(SIZES) + 2
            pool.wait_ge(setup, constants)
            pool.affine_select(out=identity[:, :], in_=identity[:, :], compare_op=ALU.not_equal, fill=1.0,
                               base=0, pattern=[[-1, P]], channel_multiplier=1).then_inc(setup, 1)
            pool.wait_ge(ids_in, 16)
            for t in range(TILES):
                for g, group in enumerate(LOOKUP_GROUPS):
                    n = t * NG + g
                    if n >= ROWS_RING:
                        pool.wait_ge(transposed, n - ROWS_RING + 1)
                    for x, slot in enumerate(group):
                        f = LOOKED_UP[slot]
                        pool.indirect_dma_start(
                            rows_sb[:, n % ROWS_RING, x, :], None, tables[f],
                            bass.IndirectOffsetOnAxis(ap=ids_sb[:, t, f:f + 1], axis=0),
                        ).then_inc(gathered[t][g], 16)

        SETUP = len(SIZES) + 3
        READS = 3

        def wait_for_room(engine, t, c):
            half_steps = STEPS[t] // 2
            if t in WHOLE and t >= 2 and c == 0:
                engine.wait_ge(square_done, t - 1)
            if t in SPLIT[1:] and c % half_steps == 0:
                engine.wait_ge(summed, 2 * SPLIT.index(t) - 1 + c // half_steps)

        def halves(width):
            return (0, width // 2), (width // 2, width)

        @block.scalar
        def _(act):
            def split_hi(k, half):
                r = k % TABLE_RING
                first, last = halves(CHUNKS[k] * DIM)[half]
                if half == 0:
                    act.wait_ge(table_in[k % RAW_RING], 16 * (k // RAW_RING + 1))
                if k >= TABLE_RING:
                    before = k - TABLE_RING
                    act.wait_ge(chunk_used, FIRST_CHUNK[before] + min(last // DIM, CHUNKS[before]))
                act.activation(hi[:, r, first:last], raw[:, k % RAW_RING, first:last], ACT.Copy).then_inc(hi_done, 1)

            def read_selected(k):
                act.wait_ge(chunk_used, FIRST_CHUNK[k + 1])
                act.activation(wholeT[:, :, :, :, NL + k].rearrange("p t g s -> p t s g"),
                               gram[:, k % 2, 0, 0:SPLIT_COLUMNS].rearrange(
                                   "p (t s g) -> p t s g", t=len(WHOLE), s=SIDE),
                               ACT.Copy).then_inc(selected_read, 1)
                for part in range(2 if k < NS - 1 else 1):
                    act.activation(splitT[:, :, :, part, :, NL + k].rearrange("p t g s -> p t s g"),
                                   gram[:, k % 2, part, SPLIT_COLUMNS:BATCH].rearrange(
                                       "p (t s g) -> p t s g", t=len(SPLIT), s=SIDE),
                                   ACT.Copy).then_inc(selected_read, 1)

            def read_lookups(t, g):
                group = LOOKUP_GROUPS[g]
                act.wait_ge(transposed, t * NG + g + 1)
                high = wholeT[:, WHOLE.index(t)] if t in WHOLE else splitT[:, SPLIT.index(t), :, 0]
                act.activation(high[:, :, :, group[0]:group[-1] + 1].rearrange("p g s f -> p f s g"),
                               rowsT[:, (t * NG + g) % 2, 0:len(group) * P].rearrange(
                                   "p (f s g) -> p f s g", s=SIDE, g=GROUPS),
                               ACT.Copy).then_inc(lookups_read, 1)

            for k in range(LOADED_BY_ACT):
                f, n = SELECTED[k], CHUNKS[k]
                act.dma_start(raw[:, k, 0:n * DIM],
                              tables[f].rearrange("(p c) d -> p (c d)", c=n)).then_inc(table_in[k], 16)

            def select(k):
                act.wait_ge(ids_all_in[k % IDS_RING], 16 * (k // IDS_RING + 1))
                size = SIZES.index(CHUNKS[k])
                for c in range(CHUNKS[k] - BY_ACT[k], CHUNKS[k]):
                    n = FIRST_ACT[k + 1] - CHUNKS[k] + c
                    if n >= ACT_RING:
                        act.wait_ge(chunk_used, ACT_CHUNKS[n - ACT_RING] + 1)
                    act.activation(onehot_act[:, n % ACT_RING, :], ids_all[:, k % IDS_RING, :], ACT.Abs,
                                   bias=minus[:, size, c:c + 1]).then_inc(distance_done, 1)
                    act.wait_ge(distance_done, n + 1)
                    act.activation(onehot_act[:, n % ACT_RING, :], onehot_act[:, n % ACT_RING, :], ACT.Relu,
                                   bias=1.0, scale=-1.0).then_inc(onehot_act_done, 1)

            def pad_low(t):
                zeros = zero[:, 0:1].unsqueeze(2).unsqueeze(3).broadcast_to([P, GROUPS, SIDE, QUAD - NF])
                act.activation(splitT[:, t, :, 1, :, NF:QUAD], zeros, ACT.Copy).then_inc(low_padded, 1)

            for k in range(TABLE_RING):
                split_hi(k, 0)
                split_hi(k, 1)
            act.wait_ge(number_done, len(SIZES))
            for n, chunks in enumerate(SIZES):
                act.activation(minus[:, n, 0:chunks], number[:, n, 0:chunks], ACT.Copy,
                               scale=-1.0).then_inc(negated, 1)
            act.wait_ge(negated, len(SIZES))
            select(0)
            for step in SCHEDULE:
                if step[0] == "select":
                    if step[1] + 1 < NS:
                        select(step[1] + 1)
                    if step[1] + 2 < NS:
                        split_hi(step[1] + 2, 0)
                    read_selected(step[1])
                    if step[1] + 2 < NS:
                        split_hi(step[1] + 2, 1)
                    if step[1] - PAD_FROM in range(len(SPLIT)):
                        pad_low(step[1] - PAD_FROM)
                elif step[0] == "transpose":
                    read_lookups(step[1], step[2])
                elif step[0] == "gram":
                    _, t, c = step
                    n = FIRST_STEP[t] + c
                    act.wait_ge(gram_full, n + 1)
                    wait_for_room(act, t, c)
                    for q in range(ACT_QUADS):
                        act.activation(block_out(t, c, q), block_in(t, n, q), ACT.Copy).then_inc(blocks_act, 1)
                elif step[0] == "features":
                    t = step[1]
                    act.wait_ge(featsT_full, t + 1)
                    if t:
                        act.wait_ge(l1_full, 2 * t)
                    act.activation(featsT[:, :], features_bank(t)[:, 0:K1 * P], ACT.Copy).then_inc(featsT_done, 1)
                elif step[0] == "layer1":
                    _, t, half = step
                    act.wait_ge(w_in, 16 * 5)
                    if t and half == 0:
                        act.wait_ge(l2_full, K3 * t)
                    act.wait_ge(l1_full, 2 * t + half + 1)
                    for m in range(2 * half, 2 * half + 2):
                        act.activation(h1T[:, m * P:(m + 1) * P], layer_bank(t, half)[:, (m % 2) * P:(m % 2 + 1) * P],
                                       ACT.Relu, bias=b1_sb[:, m:m + 1]).then_inc(h1_done, 1)
                elif step[0] == "layer2":
                    _, t, m = step
                    if t and m == 0:
                        act.wait_ge(l3_full, t)
                    act.wait_ge(l2_full, K3 * t + m + 1)
                    act.activation(h2T[:, m * P:(m + 1) * P], layer_bank(t, m)[:, 0:P], ACT.Relu,
                                   bias=b2_sb[:, m:m + 1]).then_inc(h2_done, 1)

        @block.vector
        def _(dve):
            dve.wait_ge(setup, SETUP)
            for n, chunks in enumerate(SIZES):
                dve.tensor_copy(number[:, n, 0:chunks], number_i[:, n, 0:chunks]).then_inc(number_done, 1)

            def split_lo(k):
                n, r = CHUNKS[k], k % TABLE_RING
                for h, (first, last) in enumerate(halves(n * DIM)):
                    dve.wait_ge(hi_done, 2 * k + h + 1)
                    dve.tensor_tensor(lo[:, r, first:last], raw[:, k % RAW_RING, first:last],
                                      hi[:, r, first:last], ALU.subtract).then_inc(lo_done, 1)

            def select(k):
                size = SIZES.index(CHUNKS[k])
                dve.wait_ge(ids_all_in[k % IDS_RING], 16 * (k // IDS_RING + 1))
                for c in range(CHUNKS[k] - BY_ACT[k]):
                    n = FIRST_DVE[k] + c
                    if n >= ONEHOT_RING:
                        dve.wait_ge(chunk_used, DVE_CHUNKS[n - ONEHOT_RING] + 1)
                    dve.tensor_scalar(onehot[:, n % ONEHOT_RING, :], ids_all[:, k % IDS_RING, :],
                                      number[:, size, c:c + 1], None, ALU.is_equal).then_inc(onehot_done, 1)

            dve.wait_ge(number_done, len(SIZES))
            for t in range(len(WHOLE)):
                dve.memset(wholeT[:, t, :, :, NF:QUAD], 0.0).then_inc(pad_done, 1)
            for t in range(len(SPLIT)):
                dve.memset(splitT[:, t, :, 0, :, NF:QUAD].bitcast(FP32), 0.0).then_inc(pad_done, 1)
            dve.memset(feats[:, :, FEATURES:K1 * P], 0.0).then_inc(pad_done, 1)
            for step in SCHEDULE:
                if step[0] == "select":
                    select(step[1])
                    if step[1] == 0:
                        split_lo(0)
                    if step[1] + 1 < NS:
                        split_lo(step[1] + 1)
                    else:
                        dve.wait_ge(chunk_used, FIRST_CHUNK[NS])
                        dve.tensor_copy(splitT[:, :, :, 1, :, NF - 1].rearrange("p t g s -> p t s g"),
                                        gram[:, (NS - 1) % 2, 1, SPLIT_COLUMNS:BATCH].rearrange(
                                            "p (t s g) -> p t s g", t=len(SPLIT), s=SIDE)
                                        ).then_inc(last_read, 1)
                elif step[0] == "low":
                    _, t, g = step
                    n = t * NG + g
                    slots = slice(LOOKUP_GROUPS[g][0], LOOKUP_GROUPS[g][-1] + 1)
                    dve.wait_ge(lookups_read, n + 1)
                    dve.tensor_tensor(splitT[:, SPLIT.index(t), :, 1, :, slots].rearrange("p g s f -> p f s g"),
                                      rowsT[:, n % 2, 0:len(LOOKUP_GROUPS[g]) * P].rearrange(
                                          "p (f s g) -> p f s g", s=SIDE, g=GROUPS),
                                      splitT[:, SPLIT.index(t), :, 0, :, slots].rearrange("p g s f -> p f s g"),
                                      ALU.subtract).then_inc(lookups_low, 1)
                elif step[0] == "gram":
                    _, t, c = step
                    n = FIRST_STEP[t] + c
                    half_steps = STEPS[t] // 2
                    dve.wait_ge(gram_full, n + 1)
                    wait_for_room(dve, t, c)
                    for q in range(ACT_QUADS, SIDE):
                        dve.tensor_copy(block_out(t, c, q), block_in(t, n, q)).then_inc(blocks_dve, 1)
                    if t in WHOLE or (c + 1) % half_steps:
                        continue
                    dve.wait_ge(blocks_act, ACT_QUADS * (n + 1))
                    dve.wait_ge(blocks_dve, (SIDE - ACT_QUADS) * (n + 1))
                    if t >= 2:
                        dve.wait_ge(square_done, t - 1)
                    half = slice((c + 1 - half_steps) * STEP_GROUPS[t], (c + 1) * STEP_GROUPS[t])
                    dve.scalar_tensor_tensor(sums[:, t % 2, half, :], blocks[:, half, 0, :], 0.5,
                                             blocks[:, half, 1, :], ALU.mult, ALU.add).then_inc(summed, 1)
                elif step[0] == "pack":
                    t = step[1]
                    if t in WHOLE:
                        dve.wait_ge(blocks_act, ACT_QUADS * FIRST_STEP[t + 1])
                        dve.wait_ge(blocks_dve, (SIDE - ACT_QUADS) * FIRST_STEP[t + 1])
                    else:
                        dve.wait_ge(summed, 2 * SPLIT.index(t) + 2)
                    if t:
                        dve.wait_ge(packed, len(PACKING) * t)
                    dve.transpose(square[:, 0:NF * QUAD].rearrange("p (j i) -> p j i", i=QUAD),
                                  sums[:, t % 2].rearrange("p g j -> p j g")).then_inc(square_done, 1)
                    dve.wait_ge(square_done, t + 1)
                    if t >= 2:
                        dve.wait_ge(featsT_full, t - 1)
                    for at, packing in zip(WRITTEN, PACKING):
                        count, width = packing[2:]
                        dst = feats[:, t % 2, at:at + count * width].rearrange("p (r x) -> p r x", x=width)
                        ba, ab = pair_views(square, *packing)
                        if t in WHOLE:
                            dve.tensor_copy(dst, ba).then_inc(packed, 1)
                        else:
                            dve.tensor_tensor(dst, ba, ab, ALU.add).then_inc(packed, 1)
                elif step[0] == "layer3":
                    t = step[1]
                    dve.wait_ge(l3_full, t + 1)
                    dve.tensor_copy(y_sb[:, t * P:(t + 1) * P], layer_bank(t, 0)[0:1, 0:P]).then_inc(y_done, 1)

        @block.tensor
        def _(pe):
            pe.wait_ge(setup, SETUP)

            for _ in range(WARM_UP):
                pe.matmul(rowsT[:, 1, 0:P], identity[:, :], identity[:, :], start=True, stop=True)
            for step in SCHEDULE:
                kind, t = step[0], step[1]
                if kind == "select":
                    k = t
                    r = k % TABLE_RING
                    n = CHUNKS[k]
                    if k >= 2:
                        pe.wait_ge(selected_read, READS * (k - 1))

                    def moving(c):
                        if c >= n - BY_ACT[k]:
                            q = FIRST_ACT[k + 1] - n + c
                            pe.wait_ge(onehot_act_done, q + 1)
                            return onehot_act[:, q % ACT_RING, :]
                        q = FIRST_DVE[k] + c
                        pe.wait_ge(onehot_done, q + 1)
                        return onehot[:, q % ONEHOT_RING, :]

                    def high(c, ones):
                        pe.wait_ge(hi_done, 2 * k + 1 + c // (n // 2))
                        pe.matmul(gram[:, k % 2, 0, :], hi[:, r, c * DIM:(c + 1) * DIM], ones,
                                  start=(c == 0), stop=(c == n - 1))

                    def low(c, ones):
                        pe.wait_ge(lo_done, 2 * k + 1 + c // (n // 2))
                        rows = lo[:, r, c * DIM:(c + 1) * DIM]
                        pe.matmul(gram[:, k % 2, 0, 0:SPLIT_COLUMNS], rows, ones[:, 0:SPLIT_COLUMNS],
                                  start=False, stop=False)
                        if c == n - 1:
                            high(c, ones)
                        pe.matmul(gram[:, k % 2, 1, SPLIT_COLUMNS:BATCH], rows, ones[:, SPLIT_COLUMNS:BATCH],
                                  start=(c == 0), stop=(c == n - 1)).then_inc(chunk_used, 1)

                    if k == 0:
                        for c in range(n - 1):
                            high(c, moving(c))
                        for c in range(n):
                            low(c, moving(c))
                        continue
                    for c in range(n):
                        ones = moving(c)
                        if c < n - 1:
                            high(c, ones)
                        low(c, ones)
                elif kind == "transpose":
                    g = step[2]
                    pe.wait_ge(gathered[t][g], 16 * len(LOOKUP_GROUPS[g]))
                    n = t * NG + g
                    if n >= 2:
                        pe.wait_ge(lookups_read, n - 1)
                        if (n - 2) // NG in SPLIT:
                            pe.wait_ge(lookups_low, low_groups(n - 1))
                    for x in range(len(LOOKUP_GROUPS[g])):
                        last = pe.transpose(rowsT[:, n % 2, x * P:(x + 1) * P],
                                            rows_sb[:, n % ROWS_RING, x, :], identity[:, :])
                    last.then_inc(transposed, 1)
                elif kind == "gram":
                    c = step[2]
                    n = FIRST_STEP[t] + c
                    if c == 0:
                        pe.wait_ge(pad_done, TILES + 1)
                        pe.wait_ge(low_padded, len(SPLIT))
                        pe.wait_ge(selected_read, READS * NS - 1)
                        pe.wait_ge(last_read, 1)
                        pe.wait_ge(lookups_read, NG * (t + 1))
                        if t in SPLIT:
                            pe.wait_ge(lookups_low, low_groups(NG * (t + 1)))
                    if n >= 2:
                        pe.wait_ge(blocks_act, ACT_QUADS * (n - 1))
                        pe.wait_ge(blocks_dve, (SIDE - ACT_QUADS) * (n - 1))
                    for g in range(STEP_GROUPS[t]):
                        first = c * STEP_GROUPS[t] + g
                        if t in WHOLE:
                            four = wholeT[:, WHOLE.index(t), first, :, :]
                            last = pe.matmul(gram[:, n % 2, g // 4, (g % 4) * SIDE * NF:(g % 4 + 1) * SIDE * NF],
                                             four.rearrange("p s f -> p (s f)"), four[:, :, 0:NF],
                                             start=True, stop=True)
                        else:
                            both = splitT[:, SPLIT.index(t), first].rearrange("p m s f -> p (m s f)")
                            last = pe.matmul(gram[:, n % 2, g // 2, (g % 2) * 2 * P:(g % 2 + 1) * 2 * P],
                                             both[:, 0:P], both, start=True, stop=True)
                    last.then_inc(gram_full, 1)
                elif kind == "features":
                    if 0 < t < TILES - 1:
                        pe.wait_ge(y_done, t)
                    for k in range(K1):
                        if k == K1 - 1:
                            pe.wait_ge(dense_in[t % 2], 16 * (t // 2 + 1))
                        pe.wait_ge(packed, len(PACKING) * t + PACKED_BY[k])
                        last = pe.transpose(features_bank(t)[:, k * P:(k + 1) * P],
                                            feats[:, t % 2, k * P:(k + 1) * P], identity[:, :])
                    last.then_inc(featsT_full, 1)
                elif kind == "layer1":
                    half = step[2]
                    pe.wait_ge(w_in, 16 * 5)
                    pe.wait_ge(featsT_done, t + 1)
                    for m in range(2 * half, 2 * half + 2):
                        for k in range(K1):
                            last = pe.matmul(layer_bank(t, half)[:, (m % 2) * P:(m % 2 + 1) * P],
                                             w1_sb[:, k, m * P:(m + 1) * P], featsT[:, k * P:(k + 1) * P],
                                             start=(k == 0), stop=(k == K1 - 1))
                    last.then_inc(l1_full, 1)
                elif kind == "layer2":
                    m = step[2]
                    for k in range(K2):
                        pe.wait_ge(h1_done, K2 * t + max(k + 1, 2))
                        last = pe.matmul(layer_bank(t, m)[:, 0:P], w2_sb[:, k, m * P:(m + 1) * P],
                                         h1T[:, k * P:(k + 1) * P], start=(k == 0), stop=(k == K2 - 1))
                    last.then_inc(l2_full, 1)
                elif kind == "layer3":
                    for k in range(K3):
                        pe.wait_ge(h2_done, K3 * t + k + 1)
                        last = pe.matmul(layer_bank(t, 0)[0:1, 0:P], w3_sb[:, k:k + 1], h2T[:, k * P:(k + 1) * P],
                                         start=(k == 0), stop=(k == K3 - 1))
                    last.then_inc(l3_full, 1)


def kernel(**inputs):
    import concourse.bacc as bacc
    from concourse.bass_utils import run_bass_kernel_spmd

    def columns(v):
        return np.ascontiguousarray(np.asarray(v).reshape(-1, P).T)

    w1 = np.asarray(inputs["W_top1"])
    w1_rows = np.zeros((K1 * P, H1), w1.dtype)
    w1_rows[:FEATURES] = w1[feature_rows()]
    ids = np.ascontiguousarray(inputs["ids"])
    arrays = {
        "in_dense": np.ascontiguousarray(inputs["dense_ctx"]),
        "in_ids": np.ascontiguousarray(ids.reshape(TILES, P, NF).transpose(1, 0, 2)),
        "in_ids_rows": np.ascontiguousarray(ids.T.reshape(NF, TILES, P)[:, COLUMN_TILES].reshape(NF, BATCH)),
        **{f"in_tbl_{f}": np.ascontiguousarray(inputs[f"tbl_{f}"]) for f in range(NF)},
        "in_w1": w1_rows,
        "in_b1": columns(inputs["b_top1"]),
        "in_w2": np.ascontiguousarray(inputs["W_top2"]),
        "in_b2": columns(inputs["b_top2"]),
        "in_w3": columns(inputs["W_top3"]),
    }
    nc = bacc.Bacc("TRN2", target_bir_lowering=False, num_devices=1)
    dram = {name: nc.dram_tensor(name, a.shape, mybir.dt.from_np(a.dtype), kind="ExternalInput").ap()
            for name, a in arrays.items()}
    y = nc.dram_tensor("out_y", (BATCH, 1), FP32, kind="ExternalOutput").ap()
    tower(nc, dram["in_dense"], dram["in_ids"], dram["in_ids_rows"], [dram[f"in_tbl_{f}"] for f in range(NF)],
          dram["in_w1"], dram["in_b1"], dram["in_w2"], dram["in_b2"], dram["in_w3"], y)
    return run_bass_kernel_spmd(nc, [arrays], core_ids=[0]).results[0]["out_y"]
```
